# Optimizing a Trainium2 kernel written in Bass

```python
import numpy as np
import jax
import jax.numpy as jnp

def _softmax(x, axis=-1):
    return jax.nn.softmax(x, axis=axis)

def _gelu(x):
    return jax.nn.gelu(x, approximate=True)

def _silu(x):
    return jax.nn.silu(x)

def _sigmoid(x):
    return jax.nn.sigmoid(x)

def _layernorm(x, axis=-1, eps=1e-05):
    m = jnp.mean(x, axis=axis, keepdims=True)
    v = jnp.var(x, axis=axis, keepdims=True)
    return (x - m) / jnp.sqrt(v + eps)

def _scatter_add(tgt, idx, src, axis=0):
    return tgt.at[idx].add(src)

def _segment_sum(src, seg, n):
    return jax.ops.segment_sum(src, seg, n)
kernel_name = 'mk_rec_standalone_d1_rec_r8_511369'

def setup_inputs(seed: int=0):
    np.random.seed(seed)
    _w = jnp.asarray

    def _rec_inputs():
        import jax
        import jax.numpy as jnp
        _rk = jax.random.key(seed)
        r_candidate_news_vector = -0.000392918 + 0.999932 * jax.random.normal(jax.random.fold_in(_rk, 1), (512, 64, 256), jnp.float32)
        r_clicked_news_vector = 2.81802e-05 + 1.00001 * jax.random.normal(jax.random.fold_in(_rk, 2), (512, 64, 256), jnp.float32)
        r_mask_cand = jax.random.bernoulli(jax.random.fold_in(_rk, 3), 0.5074, (512, 64))
        r_mask_hist = jax.random.bernoulli(jax.random.fold_in(_rk, 4), 0.5117, (512, 64))
        return (r_candidate_news_vector, r_clicked_news_vector, r_mask_cand, r_mask_hist)
    r_candidate_news_vector, r_clicked_news_vector, r_mask_cand, r_mask_hist = _rec_inputs()

    def _L0_rec_setup():
        import jax, jax.numpy as jnp
        import numpy as np
        B, C, H, D, HID = (1024, 64, 64, 256, 256)
        key = jax.random.key(seed)
        k1, k2, k3, k4, k5, k6, k7, k8 = jax.random.split(key, 8)
        candidate_news_vector = jax.random.normal(k1, (B, C, D), dtype=jnp.float32)
        clicked_news_vector = jax.random.normal(k2, (B, H, D), dtype=jnp.float32)
        mask_cand = jax.random.randint(k3, (B, C), 0, 2).astype(bool).at[:, 0].set(True)
        mask_hist = jax.random.randint(k4, (B, H), 0, 2).astype(bool).at[:, 0].set(True)
        s1 = 1.0 / np.sqrt(2 * D)
        s2 = 1.0 / np.sqrt(HID)
        W1 = jax.random.uniform(k5, (HID, 2 * D), minval=-s1, maxval=s1, dtype=jnp.float32)
        b1 = jax.random.uniform(k6, (HID,), minval=-s1, maxval=s1, dtype=jnp.float32)
        W2 = jax.random.uniform(k7, (1, HID), minval=-s2, maxval=s2, dtype=jnp.float32)
        b2 = jax.random.uniform(k8, (1,), minval=-s2, maxval=s2, dtype=jnp.float32)
        return {'candidate_news_vector': candidate_news_vector, 'clicked_news_vector': clicked_news_vector, 'mask_cand': mask_cand, 'mask_hist': mask_hist, 'W1': W1, 'b1': b1, 'W2': W2, 'b2': b2}
    _L0_rec_all = _L0_rec_setup()
    _L0_rec_in = {k: v for k, v in _L0_rec_all.items() if k in ('W1', 'b1', 'W2', 'b2')}
    del _L0_rec_all
    return {'r_candidate_news_vector': r_candidate_news_vector, 'r_clicked_news_vector': r_clicked_news_vector, 'r_mask_cand': r_mask_cand, 'r_mask_hist': r_mask_hist, 'L0_rec_W1': _L0_rec_in['W1'], 'L0_rec_b1': _L0_rec_in['b1'], 'L0_rec_W2': _L0_rec_in['W2'], 'L0_rec_b2': _L0_rec_in['b2']}

def reference(r_candidate_news_vector, r_clicked_news_vector, r_mask_cand, r_mask_hist, L0_rec_W1, L0_rec_b1, L0_rec_W2, L0_rec_b2):
    import jax
    import jax.numpy as jnp

    def _L0_rec_ref(candidate_news_vector, clicked_news_vector, mask_cand, mask_hist, W1, b1, W2, b2):
        import jax, jax.numpy as jnp
        import numpy as np
        B, C, H, D, HID = (1024, 64, 64, 256, 256)
        d = candidate_news_vector.shape[-1]
        w2 = W2[0]
        v_c = W1[:, :d].T @ w2
        v_h = W1[:, d:].T @ w2
        bias = jnp.dot(w2, b1) + b2[0]
        scores = jnp.einsum('bcd,d->bc', candidate_news_vector, v_c)[:, :, None] + jnp.einsum('bhd,d->bh', clicked_news_vector, v_h)[:, None, :] + bias
        neg = jnp.finfo(scores.dtype).min
        scores = jnp.where(mask_hist[:, None, :], scores, neg)
        weights = jax.nn.softmax(scores, axis=-1)
        weights = jnp.where(mask_cand[:, :, None], weights, 0.0)
        user_vector = jnp.einsum('bch,bhd->bcd', weights, clicked_news_vector)
        return user_vector
    y = _L0_rec_ref(r_candidate_news_vector, r_clicked_news_vector, r_mask_cand, r_mask_hist, L0_rec_W1, L0_rec_b1, L0_rec_W2, L0_rec_b2)
    return y

_drawn_inputs = setup_inputs


def setup_inputs(seed=0):
    import zlib

    import numpy as np

    out = dict(_drawn_inputs(seed))
    spreads = {}
    factors = {}
    for name, (base, spread) in spreads.items():
        noise = np.random.default_rng([zlib.crc32(name.encode()), seed]).standard_normal(out[name].shape)
        drawn = base * np.exp(spread * noise) if base else spread * noise
        out[name] = jnp.asarray(drawn.astype(out[name].dtype))
    for name, factor in factors.items():
        out[name] = (out[name] * factor).astype(out[name].dtype)
    return out
```

```python
from contextlib import ExitStack

import concourse.bass as bass
from concourse import mybir

ALU = mybir.AluOpType
ACT = mybir.ActivationFunctionType
F32 = mybir.dt.float32
U8 = mybir.dt.uint8
AX_X = mybir.AxisListType.X

P = 128
PAIRS = 8
UNROLL = 4
CAP = 2.0 ** 126


def candidate_attention_kernel(
    nc: bass.Bass,
    cand: bass.AP,
    clicked: bass.AP,
    mask_cand: bass.AP,
    mask_hist: bass.AP,
    w1: bass.AP,
    b1: bass.AP,
    w2: bass.AP,
    b2: bass.AP,
    identity: bass.AP,
    same_parity: bass.AP,
    place_candidate: bass.AP,
    place_batch: bass.AP,
    out: bass.AP,
):
    B, C, D = cand.shape
    H = clicked.shape[1]
    HID = w1.shape[0]
    KT = HID // P
    NPAIR = B // 2
    CHUNKS = NPAIR // PAIRS
    ROUNDS = CHUNKS // UNROLL
    EIGHTH = 2 * C * PAIRS // P
    MT = NPAIR // P
    BANKS = PAIRS // 2
    assert 2 * H == P and 2 * C == P and 2 * D == 512 and PAIRS * C == 512

    clicked_v = clicked.rearrange("(k i b) h d -> k (b h) i d", i=PAIRS, b=2)
    out_v = out.rearrange("(k i b) c d -> k (b c) i d", i=PAIRS, b=2)
    cand_v = cand.rearrange("(k n) (q j) d -> k (n q) (j d)", n=2 * PAIRS, j=EIGHTH)

    with ExitStack() as ctx:
        def sb(name, shape, dt=F32):
            return ctx.enter_context(nc.sbuf_tensor(name, shape, dt))

        def ps(name):
            return ctx.enter_context(nc.psum_tensor(name, [P, 512], F32))

        def sem(name):
            return ctx.enter_context(nc.semaphore(name))

        clicked_sb = [sb(f"clicked{u}", [P, PAIRS, D]) for u in range(UNROLL)]
        cand_sb = [sb(f"cand{u}", [P, EIGHTH, D]) for u in range(UNROLL)]
        out_sb = [sb(f"out{u}", [P, PAIRS, D]) for u in range(UNROLL)]

        ident = sb("ident", [P, P])
        parity = sb("parity", [P, P])
        neg_place_c = sb("neg_place_c", [P, PAIRS, 8])
        place_b = sb("place_b", [PAIRS, PAIRS, 2, 8])
        ones_row = sb("ones_row", [1, P])
        ones_col = sb("ones_col", [P, 1])
        w1_sb = sb("w1_sb", [P, KT, 2 * D])
        w2_sb = sb("w2_sb", [P, KT])
        w2_wide = sb("w2_wide", [P, KT, P])
        b1_sb = sb("b1_sb", [P, KT])
        b2_sb = sb("b2_sb", [1, 1])
        v_sb = sb("v_sb", [P, 2 * D])
        bias_sb = sb("bias_sb", [P, 1])
        hist_u8 = sb("hist_u8", [P, MT, P], U8)
        keep_u8 = sb("keep_u8", [P, MT, P], U8)
        hist_f = sb("hist_f", [P, MT, P])
        keep_f = sb("keep_f", [P, MT, P])
        cap = sb("cap", [P, NPAIR])
        keep = sb("keep", [P, NPAIR])

        product = sb("product", [P, PAIRS, D])
        s_h = [sb(f"s_h{u}", [P, PAIRS]) for u in range(2)]
        s_hm = [sb(f"s_hm{u}", [P, PAIRS]) for u in range(2)]
        s_c = [sb(f"s_c{u}", [P, EIGHTH]) for u in range(2)]
        top = [sb(f"top{u}", [PAIRS, 2]) for u in range(2)]
        top_placed = [sb(f"top_placed{u}", [PAIRS, PAIRS, 2, 8]) for u in range(2)]
        top_c = [sb(f"top_c{u}", [P, 1]) for u in range(2)]
        shift = [sb(f"shift{u}", [P, EIGHTH]) for u in range(2)]
        shift_placed = [sb(f"shift_placed{u}", [P, PAIRS, 8, EIGHTH]) for u in range(2)]
        weights = [sb(f"weights{u}", [P, PAIRS, P]) for u in range(2)]
        inv_sum = [sb(f"inv_sum{u}", [P, PAIRS]) for u in range(2)]
        scale = [sb(f"scale{u}", [P, PAIRS]) for u in range(2)]

        user_ps = [ps(f"user_ps{n}") for n in range(BANKS)]
        exponent_ps = ps("exponent_ps")
        turned_ps = ps("turned_ps")
        top_ps = ps("top_ps")
        sum_ps = ps("sum_ps")

        clicked_in = [sem(f"clicked_in{u}") for u in range(UNROLL)]
        cand_in = [sem(f"cand_in{u}") for u in range(UNROLL)]
        stored = [sem(f"stored{u}") for u in range(UNROLL)]
        weights_in = sem("weights_in")
        consts_in = sem("consts_in")
        masks_in = sem("masks_in")
        zeroed = sem("zeroed")
        w2_ready = sem("w2_ready")
        v_ready = sem("v_ready")
        v_copied = sem("v_copied")
        masks_cast = sem("masks_cast")
        masks_turned = sem("masks_turned")
        masks_ready = sem("masks_ready")
        h_dots = sem("h_dots")
        c_dots = sem("c_dots")
        h_masked = sem("h_masked")
        h_turned = sem("h_turned")
        top_found = sem("top_found")
        top_spread = sem("top_spread")
        top_ready = sem("top_ready")
        top_copied = sem("top_copied")
        shifted = sem("shifted")
        placed = sem("placed")
        exponents = sem("exponents")
        exp_done = sem("exp_done")
        sums_ready = sem("sums_ready")
        inverted = sem("inverted")
        scale_ready = sem("scale_ready")
        users_ready = sem("users_ready")
        users_taken = sem("users_taken")

        block = ctx.enter_context(nc.Block())

        @block.sync
        def _(sp):
            sp.dma_start(w2_sb[:], w2.rearrange("a (p t) -> (a p) t", t=KT)).then_inc(weights_in, 16)
            sp.dma_start(w1_sb[:], w1.rearrange("(p t) n -> p t n", t=KT)).then_inc(weights_in, 16)
            sp.dma_start(b1_sb[:], b1.rearrange("(p t) -> p t", t=KT)).then_inc(weights_in, 16)
            sp.dma_start(b2_sb[:], b2.rearrange("(a n) -> a n", a=1)).then_inc(weights_in, 16)

            def load(k, u, again):
                if again:
                    sp.wait_ge(users_ready, BANKS * (k - UNROLL + 1))
                sp.dma_start(clicked_sb[u][:], clicked_v[k]).then_inc(clicked_in[u], 16)
                if again:
                    sp.wait_ge(c_dots, k - UNROLL + 1)
                sp.dma_start(cand_sb[u][:], cand_v[k]).then_inc(cand_in[u], 16)

            def store(k, u):
                sp.wait_ge(users_taken, BANKS * (k + 1))
                sp.dma_start(out_v[k], out_sb[u][:]).then_inc(stored[u], 16)

            load(0, 0, False)
            sp.dma_start(ident[:], identity).then_inc(consts_in, 16)
            sp.dma_start(parity[:], same_parity).then_inc(consts_in, 16)
            sp.dma_start(neg_place_c[:], place_candidate).then_inc(consts_in, 16)
            sp.dma_start(place_b[:], place_batch).then_inc(consts_in, 16)
            half = mask_hist.rearrange("(t p b) h -> p t (b h)", p=P, b=2)
            sp.dma_start(hist_u8[:], half).then_inc(masks_in, 16)
            half = mask_cand.rearrange("(t p b) h -> p t (b h)", p=P, b=2)
            sp.dma_start(keep_u8[:], half).then_inc(masks_in, 16)
            for u in range(1, UNROLL):
                load(u, u, False)
            with sp.Fori(0, ROUNDS - 1) as g:
                for u in range(UNROLL):
                    k = g * UNROLL + u
                    load(k + UNROLL, u, True)
                    store(k, u)
            for u in range(UNROLL):
                store(CHUNKS - UNROLL + u, u)
            for u in range(UNROLL):
                sp.wait_ge(stored[u], 16 * ROUNDS)

        @block.gpsimd
        def _(pool):
            for u in range(2):
                nc.gpsimd.memset(weights[u][:], 0.0).then_inc(zeroed, 1)

        @block.vector
        def _(dve):
            nc.vector.memset(ones_row[:], 1.0)
            nc.vector.memset(ones_col[:], 1.0)
            dve.wait_ge(weights_in, 64)
            nc.vector.tensor_copy(w2_wide[:], w2_sb[:].unsqueeze(2).to_broadcast([P, KT, P])).then_inc(w2_ready, 1)
            dve.wait_ge(v_ready, 1)
            nc.vector.tensor_copy(v_sb[:], exponent_ps[:]).then_inc(v_copied, 1)
            nc.vector.tensor_copy(bias_sb[:], top_ps[:, 0:1]).then_inc(v_copied, 1)
            dve.wait_ge(masks_in, 32)
            nc.vector.tensor_copy(hist_f[:], hist_u8[:]).then_inc(masks_cast, 1)
            nc.vector.tensor_copy(keep_f[:], keep_u8[:]).then_inc(masks_cast, 1)
            dve.wait_ge(masks_turned, 2 * MT)
            nc.vector.tensor_scalar(cap[:], user_ps[0][:, 0:NPAIR], 0.5, 2.0 * CAP, ALU.subtract,
                                    ALU.mult).then_inc(masks_ready, 1)
            nc.vector.tensor_copy(keep[:], user_ps[1][:, 0:NPAIR]).then_inc(masks_ready, 1)
            dve.wait_ge(v_copied, 2)
            dve.wait_ge(masks_ready, 2)

            def dot(product, data, j, v0, total, u, init):
                return nc.vector.tensor_tensor_reduce(
                    out=product[:, j, :], in0=data[:, j, :], in1=v_sb[:, v0:v0 + D], scale=1.0, scalar=init,
                    op0=ALU.mult, op1=ALU.add, accum_out=total[u][:, j:j + 1])

            def clicked_dots(k, u, lo, hi):
                if lo == 0:
                    dve.wait_ge(clicked_in[u], rnd(k, u))
                for j in range(lo, hi):
                    last = dot(product, clicked_sb[u], j, D, s_h, u % 2, 0.0)
                if hi == PAIRS:
                    last.then_inc(h_dots, 1)

            def rnd(k, u):
                return (k - u) * (16 // UNROLL) + 16

            def masked(k, u):
                dve.wait_ge(h_dots, k + 1)
                nc.vector.tensor_tensor(s_hm[u % 2][:], s_h[u % 2][:], cap[:, bass.ds(k * PAIRS, PAIRS)],
                                        ALU.min).then_inc(h_masked, 1)

            def cand_dots(k, u, lo, hi):
                if lo == 0:
                    dve.wait_ge(cand_in[u], rnd(k, u))
                for j in range(lo, hi):
                    last = dot(cand_sb[u], cand_sb[u], j, 0, s_c, u % 2, bias_sb[:, 0:1])
                if hi == EIGHTH:
                    last.then_inc(c_dots, 1)

            def batch_top(k, u):
                dve.wait_ge(h_turned, k + 1)
                nc.vector.tensor_reduce(top[u % 2][:], turned_ps[0:PAIRS, 0:P].rearrange("i (b h) -> i b h", b=2),
                                        AX_X, ALU.max).then_inc(top_found, 1)
                dve.wait_ge(top_found, k + 1)
                nc.vector.tensor_tensor(
                    top_placed[u % 2][:].rearrange("k i b q -> k i (b q)").rearrange("k i (b q) -> k i b q", b=2),
                    place_b[:], top[u % 2][:].unsqueeze(1).unsqueeze(3).to_broadcast([PAIRS, PAIRS, 2, 8]),
                    ALU.mult).then_inc(top_spread, 1)

            def candidate_shift(k, u):
                dve.wait_ge(top_ready, k + 1)
                nc.vector.tensor_copy(top_c[u % 2][:], top_ps[:, 0:1]).then_inc(top_copied, 1)
                dve.wait_ge(top_copied, k + 1)
                dve.wait_ge(c_dots, k + 1)
                nc.vector.scalar_tensor_tensor(out=shift[u % 2][:], in0=s_c[u % 2][:], scalar=top_c[u % 2][:, 0:1],
                                               in1=s_c[u % 2][:], op0=ALU.add, op1=ALU.subtract).then_inc(shifted, 1)
                dve.wait_ge(shifted, k + 1)
                nc.vector.tensor_tensor(
                    shift_placed[u % 2][:],
                    neg_place_c[:].unsqueeze(3).to_broadcast([P, PAIRS, 8, EIGHTH]),
                    shift[u % 2][:].unsqueeze(1).unsqueeze(1).to_broadcast([P, PAIRS, 8, EIGHTH]),
                    ALU.mult).then_inc(placed, 1)

            def row_scale(k, u):
                dve.wait_ge(sums_ready, k + 1)
                nc.vector.reciprocal(inv_sum[u % 2][:], sum_ps[:, 0:PAIRS]).then_inc(inverted, 1)
                dve.wait_ge(inverted, k + 1)
                nc.vector.tensor_tensor(scale[u % 2][:], inv_sum[u % 2][:], keep[:, bass.ds(k * PAIRS, PAIRS)],
                                        ALU.mult).then_inc(scale_ready, 1)

            def step(k, u, behind1, behind2):
                clicked_dots(k, u, 0, 4)
                if behind2:
                    row_scale(k - 2, u - 2)
                clicked_dots(k, u, 4, PAIRS)
                masked(k, u)
                if behind1:
                    candidate_shift(k - 1, u - 1)
                cand_dots(k, u, 0, 4)
                batch_top(k, u)
                cand_dots(k, u, 4, EIGHTH)

            dve.wait_ge(consts_in, 64)
            for u in range(UNROLL):
                step(u, u, u >= 1, u >= 2)
            with dve.Fori(1, ROUNDS) as g:
                for u in range(UNROLL):
                    step(g * UNROLL + u, u, True, True)
            row_scale(CHUNKS - 2, 0)
            candidate_shift(CHUNKS - 1, 1)
            row_scale(CHUNKS - 1, 1)

        @block.tensor
        def _(pe):
            pe.wait_ge(w2_ready, 1)
            for t in range(KT):
                nc.tensor.matmul(exponent_ps[:], w2_wide[:, t, :], w1_sb[:, t, :], start=(t == 0), stop=(t == KT - 1))
            for t in range(KT):
                nc.tensor.matmul(top_ps[:, 0:1], w2_wide[:, t, :], b1_sb[:, t:t + 1], start=(t == 0), stop=False)
            nc.tensor.matmul(top_ps[:, 0:1], ones_row[:], b2_sb[:], start=False, stop=True).then_inc(v_ready, 1)
            pe.wait_ge(consts_in, 64)
            pe.wait_ge(masks_cast, 2)
            for n, flat in enumerate((hist_f, keep_f)):
                for t in range(MT):
                    nc.tensor.transpose(user_ps[n][:, t * P:(t + 1) * P], flat[:, t, :], ident[:]).then_inc(masks_turned, 1)
            pe.wait_ge(masks_ready, 2)

            def turn_scores(k, u):
                pe.wait_ge(h_masked, k + 1)
                nc.tensor.transpose(turned_ps[0:PAIRS, 0:P], s_hm[u % 2][:], ident[:]).then_inc(h_turned, 1)

            def spread_top(k, u):
                pe.wait_ge(top_spread, k + 1)
                nc.tensor.matmul(top_ps[:, 0:1], top_placed[u % 2][:].rearrange("k i b q -> k (i b q)"),
                                 ones_col[0:PAIRS, :], start=True, stop=True).then_inc(top_ready, 1)

            def spread_exponents(k, u, again):
                pe.wait_ge(placed, k + 1)
                if again:
                    pe.wait_ge(exp_done, k)
                nc.tensor.matmul(exponent_ps[:], parity[:], shift_placed[u % 2][:].rearrange("p i q j -> p (i q j)"),
                                 start=True, stop=False)
                nc.tensor.matmul(exponent_ps[:], ident[:], s_hm[u % 2][:].unsqueeze(2).to_broadcast([P, PAIRS, C]),
                                 start=False, stop=True).then_inc(exponents, 1)

            def products(k, u, again):
                pe.wait_ge(exp_done, k + 1)
                if again:
                    pe.wait_ge(inverted, k)
                for i in range(PAIRS):
                    last = nc.tensor.matmul(sum_ps[:, i:i + 1], weights[u % 2][:, i, :], ones_col[:], start=True, stop=True)
                last.then_inc(sums_ready, 1)
                for n in range(BANKS):
                    if again:
                        pe.wait_ge(users_taken, BANKS * (k - 1) + n + 1)
                    for i in (2 * n, 2 * n + 1):
                        last = nc.tensor.matmul(user_ps[n][:, (i % 2) * D:(i % 2 + 1) * D], weights[u % 2][:, i, :],
                                                clicked_sb[u][:, i, :], start=True, stop=True)
                    last.then_inc(users_ready, 1)

            def step(k, u, behind1, behind2):
                turn_scores(k, u)
                if behind1:
                    spread_exponents(k - 1, u - 1, behind2)
                spread_top(k, u)
                if behind1:
                    products(k - 1, (u - 1) % UNROLL, behind2)

            for u in range(UNROLL):
                step(u, u, u >= 1, u >= 2)
            with pe.Fori(1, ROUNDS) as g:
                for u in range(UNROLL):
                    step(g * UNROLL + u, u, True, True)
            spread_exponents(CHUNKS - 1, UNROLL - 1, True)
            products(CHUNKS - 1, UNROLL - 1, True)

        @block.scalar
        def _(act):
            def exponentials(k, u):
                act.wait_ge(exponents, k + 1)
                e = exponent_ps[:].rearrange("p (i c) -> p i c", c=C)
                nc.scalar.activation(weights[u % 2][0:H, :, 0:C], e[0:H], ACT.Exp)
                nc.scalar.activation(weights[u % 2][H:P, :, C:2 * C], e[H:P], ACT.Exp).then_inc(exp_done, 1)

            def take_users(k, u, again):
                act.wait_ge(scale_ready, k + 1)
                if again is not None:
                    act.wait_ge(stored[u], again)
                for n in range(BANKS):
                    act.wait_ge(users_ready, BANKS * k + n + 1)
                    for i in (2 * n, 2 * n + 1):
                        last = nc.scalar.activation(out_sb[u][:, i, :], user_ps[n][:, (i % 2) * D:(i % 2 + 1) * D],
                                                    ACT.Copy, scale=scale[u % 2][:, i:i + 1])
                    last.then_inc(users_taken, 1)

            act.wait_ge(zeroed, 2)
            exponentials(0, 0)
            for u in range(UNROLL):
                exponentials(u + 1, (u + 1) % UNROLL)
                take_users(u, u, None)
            with act.Fori(1, ROUNDS - 1) as g:
                for u in range(UNROLL):
                    exponentials(g * UNROLL + u + 1, (u + 1) % UNROLL)
                    take_users(g * UNROLL + u, u, 16 * g)
            for u in range(UNROLL):
                k = (ROUNDS - 1) * UNROLL + u
                if k + 1 < CHUNKS:
                    exponentials(k + 1, u + 1)
                take_users(k, u, 16 * (ROUNDS - 1))


_INS = ["r_candidate_news_vector", "r_clicked_news_vector", "r_mask_cand", "r_mask_hist",
        "L0_rec_W1", "L0_rec_b1", "L0_rec_W2", "L0_rec_b2"]


def _placements():
    import numpy as np

    p = np.arange(P)
    ident = np.eye(P, dtype=np.float32)
    parity = (((p[:, None] // 8) % 2) == (p[None, :] // 64)).astype(np.float32)
    place_c = -((p[:, None, None] // 16 == np.arange(PAIRS)[None, :, None])
                & (p[:, None, None] % 8 == np.arange(8)[None, None, :])).astype(np.float32)
    place_b = np.zeros((PAIRS, PAIRS, 2, 8), np.float32)
    place_b[np.arange(PAIRS), np.arange(PAIRS)] = 1.0
    return {"identity": ident, "same_parity": parity, "place_candidate": place_c, "place_batch": place_b}


def kernel(**inputs):
    import numpy as np
    import concourse.bacc as bacc
    from concourse import mybir as _mybir
    from concourse.bass_utils import run_bass_kernel_spmd

    nc = bacc.Bacc("TRN2", target_bir_lowering=False, num_devices=1)
    arrays, args = {}, []
    for name, a in [(n, inputs[n]) for n in _INS] + list(_placements().items()):
        a = np.ascontiguousarray(a)
        arrays[f"in_{name}_dram"] = a
        args.append(nc.dram_tensor(f"in_{name}_dram", a.shape, _mybir.dt.from_np(a.dtype), kind="ExternalInput").ap())
    shape = inputs["r_candidate_news_vector"].shape
    args.append(nc.dram_tensor("out_0_dram", shape, F32, kind="ExternalOutput").ap())
    candidate_attention_kernel(nc, *args)
    r = run_bass_kernel_spmd(nc, [arrays], core_ids=[0])
    return r.results[0]["out_0_dram"]
```

```python
from contextlib import ExitStack

import concourse.bass as bass
from concourse import mybir

ALU = mybir.AluOpType
ACT = mybir.ActivationFunctionType
F32 = mybir.dt.float32
U8 = mybir.dt.uint8
AX_X = mybir.AxisListType.X

P = 128
PAIRS = 8
UNROLL = 8
CAND_RING = 4
CAP = 2.0 ** 126


def candidate_attention_kernel(
    nc: bass.Bass,
    cand: bass.AP,
    clicked: bass.AP,
    mask_cand: bass.AP,
    mask_hist: bass.AP,
    w1: bass.AP,
    b1: bass.AP,
    w2: bass.AP,
    b2: bass.AP,
    identity: bass.AP,
    same_parity: bass.AP,
    place_candidate: bass.AP,
    place_batch: bass.AP,
    out: bass.AP,
):
    B, C, D = cand.shape
    H = clicked.shape[1]
    HID = w1.shape[0]
    KT = HID // P
    NPAIR = B // 2
    CHUNKS = NPAIR // PAIRS
    ROUNDS = CHUNKS // UNROLL
    EIGHTH = 2 * C * PAIRS // P
    MT = NPAIR // P
    BANKS = PAIRS // 2
    assert 2 * H == P and 2 * C == P and 2 * D == 512 and PAIRS * C == 512

    clicked_v = clicked.rearrange("(k i b) h d -> k (b h) i d", i=PAIRS, b=2)
    out_v = out.rearrange("(k i b) c d -> k (b c) i d", i=PAIRS, b=2)
    cand_v = cand.rearrange("(k n) (q j) d -> k (n q) (j d)", n=2 * PAIRS, j=EIGHTH)

    with ExitStack() as ctx:
        def sb(name, shape, dt=F32):
            return ctx.enter_context(nc.sbuf_tensor(name, shape, dt))

        def ps(name):
            return ctx.enter_context(nc.psum_tensor(name, [P, 512], F32))

        def sem(name):
            return ctx.enter_context(nc.semaphore(name))

        clicked_sb = [sb(f"clicked{u}", [P, PAIRS, D]) for u in range(UNROLL)]
        cand_sb = [sb(f"cand{u}", [P, EIGHTH, D]) for u in range(CAND_RING)]
        out_sb = [sb(f"out{u}", [P, PAIRS, D]) for u in range(UNROLL)]

        ident = sb("ident", [P, P])
        parity = sb("parity", [P, P])
        neg_place_c = sb("neg_place_c", [P, PAIRS, 8])
        place_b = sb("place_b", [PAIRS, PAIRS, 2, 8])
        ones_row = sb("ones_row", [1, P])
        ones_col = sb("ones_col", [P, 1])
        warm = sb("warm", [1, 1])
        w1_sb = sb("w1_sb", [P, KT, 2 * D])
        w2_sb = sb("w2_sb", [P, KT])
        w2_wide = sb("w2_wide", [P, KT, P])
        b1_sb = sb("b1_sb", [P, KT])
        b2_sb = sb("b2_sb", [1, 1])
        v_sb = sb("v_sb", [P, 2 * D])
        bias_sb = sb("bias_sb", [P, 1])
        hist_u8 = sb("hist_u8", [P, MT, P], U8)
        keep_u8 = sb("keep_u8", [P, MT, P], U8)
        hist_f = sb("hist_f", [P, MT, P])
        keep_f = sb("keep_f", [P, MT, P])
        cap = sb("cap", [P, NPAIR])
        keep = sb("keep", [P, NPAIR])

        product = sb("product", [P, PAIRS, D])
        s_h = [sb(f"s_h{u}", [P, PAIRS]) for u in range(2)]
        s_hm = [sb(f"s_hm{u}", [P, PAIRS]) for u in range(2)]
        s_c = [sb(f"s_c{u}", [P, EIGHTH]) for u in range(2)]
        top = [sb(f"top{u}", [PAIRS, 2]) for u in range(2)]
        top_placed = [sb(f"top_placed{u}", [PAIRS, PAIRS, 2, 8]) for u in range(2)]
        shift = [sb(f"shift{u}", [P, EIGHTH]) for u in range(2)]
        shift_placed = [sb(f"shift_placed{u}", [P, PAIRS, 8, EIGHTH]) for u in range(2)]
        weights = [sb(f"weights{u}", [P, PAIRS, P]) for u in range(2)]
        inv_sum = [sb(f"inv_sum{u}", [P, PAIRS]) for u in range(2)]
        scale = [sb(f"scale{u}", [P, PAIRS]) for u in range(2)]

        user_ps = [ps(f"user_ps{n}") for n in range(BANKS)]
        exponent_ps = ps("exponent_ps")
        turned_ps = ps("turned_ps")
        top_ps = ps("top_ps")
        sum_ps = ps("sum_ps")

        clicked_in = [sem(f"clicked_in{u}") for u in range(UNROLL)]
        cand_in = [sem(f"cand_in{u}") for u in range(CAND_RING)]
        stored = [sem(f"stored{u}") for u in range(UNROLL)]
        weights_in = sem("weights_in")
        consts_in = sem("consts_in")
        masks_in = sem("masks_in")
        zeroed = sem("zeroed")
        ones_ready = sem("ones_ready")
        w2_ready = sem("w2_ready")
        v_ready = sem("v_ready")
        v_copied = sem("v_copied")
        masks_cast = sem("masks_cast")
        masks_turned = sem("masks_turned")
        masks_ready = sem("masks_ready")
        h_dots = sem("h_dots")
        c_dots = sem("c_dots")
        h_masked = sem("h_masked")
        h_turned = sem("h_turned")
        top_found = sem("top_found")
        top_spread = sem("top_spread")
        top_ready = sem("top_ready")
        shifted = sem("shifted")
        placed = sem("placed")
        exponents = sem("exponents")
        exp_done = sem("exp_done")
        sums_ready = sem("sums_ready")
        inverted = sem("inverted")
        scale_ready = sem("scale_ready")
        users_ready = sem("users_ready")
        users_taken = sem("users_taken")

        block = ctx.enter_context(nc.Block())

        @block.sync
        def _(sp):
            sp.dma_start(w2_sb[:], w2.rearrange("a (p t) -> (a p) t", t=KT)).then_inc(weights_in, 16)
            sp.dma_start(w1_sb[:], w1.rearrange("(p t) n -> p t n", t=KT)).then_inc(weights_in, 16)
            sp.dma_start(b1_sb[:], b1.rearrange("(p t) -> p t", t=KT)).then_inc(weights_in, 16)
            sp.dma_start(b2_sb[:], b2.rearrange("(a n) -> a n", a=1)).then_inc(weights_in, 16)

            def load_clicked(k, u, again):
                if again:
                    sp.wait_ge(users_ready, BANKS * (k - UNROLL + 1))
                sp.dma_start(clicked_sb[u][:], clicked_v[k]).then_inc(clicked_in[u], 16)

            def load_cand(k, u, again):
                if again:
                    sp.wait_ge(c_dots, k - CAND_RING + 1)
                sp.dma_start(cand_sb[u % CAND_RING][:], cand_v[k]).then_inc(cand_in[u % CAND_RING], 16)

            def store(k, u):
                sp.wait_ge(users_taken, BANKS * (k + 1))
                sp.dma_start(out_v[k], out_sb[u][:]).then_inc(stored[u], 16)

            load_clicked(0, 0, False)
            half = mask_hist.rearrange("(t p b) h -> p t (b h)", p=P, b=2)
            sp.dma_start(hist_u8[:], half).then_inc(masks_in, 16)
            half = mask_cand.rearrange("(t p b) h -> p t (b h)", p=P, b=2)
            sp.dma_start(keep_u8[:], half).then_inc(masks_in, 16)
            sp.dma_start(ident[:], identity).then_inc(consts_in, 16)
            sp.dma_start(parity[:], same_parity).then_inc(consts_in, 16)
            sp.dma_start(neg_place_c[:], place_candidate).then_inc(consts_in, 16)
            sp.dma_start(place_b[:], place_batch).then_inc(consts_in, 16)
            load_cand(0, 0, False)
            for u in range(1, UNROLL):
                load_clicked(u, u, False)
                load_cand(u, u, u >= CAND_RING)
            with sp.Fori(0, ROUNDS - 1) as g:
                for u in range(UNROLL):
                    k = g * UNROLL + u
                    load_clicked(k + UNROLL, u, True)
                    load_cand(k + UNROLL, u, True)
                    store(k, u)
            for u in range(UNROLL):
                store(CHUNKS - UNROLL + u, u)
            for u in range(UNROLL):
                sp.wait_ge(stored[u], 16 * ROUNDS)

        @block.gpsimd
        def _(pool):
            for u in range(2):
                nc.gpsimd.memset(weights[u][:], 0.0).then_inc(zeroed, 1)
            pool.wait_ge(masks_in, 32)
            nc.gpsimd.tensor_copy(hist_f[:], hist_u8[:]).then_inc(masks_cast, 1)
            nc.gpsimd.tensor_copy(keep_f[:], keep_u8[:]).then_inc(masks_cast, 1)

        @block.vector
        def _(dve):
            nc.vector.memset(ones_row[:], 1.0)
            nc.vector.memset(ones_col[:], 1.0).then_inc(ones_ready, 1)
            dve.wait_ge(weights_in, 64)
            nc.vector.tensor_copy(w2_wide[:], w2_sb[:].unsqueeze(2).to_broadcast([P, KT, P])).then_inc(w2_ready, 1)
            dve.wait_ge(v_ready, 1)
            nc.vector.tensor_copy(v_sb[:, D:2 * D], exponent_ps[:, 0:D]).then_inc(v_copied, 1)
            dve.wait_ge(v_copied, 1)

            def slot_filled(k, u, ring):
                return (k - u % ring) * (16 // ring) + 16

            def clicked_dots(k, u, lo, hi):
                if lo == 0:
                    dve.wait_ge(clicked_in[u], slot_filled(k, u, UNROLL))
                for j in range(lo, hi):
                    last = nc.vector.tensor_tensor_reduce(
                        out=product[:, j, :], in0=clicked_sb[u][:, j, :], in1=v_sb[:, D:2 * D], scale=1.0, scalar=0.0,
                        op0=ALU.mult, op1=ALU.add, accum_out=s_h[u % 2][:, j:j + 1])
                if hi == PAIRS:
                    last.then_inc(h_dots, 1)

            def cand_dots(k, u, lo, hi):
                if lo == 0:
                    dve.wait_ge(cand_in[u % CAND_RING], slot_filled(k, u, CAND_RING))
                rows = cand_sb[u % CAND_RING]
                for j in range(lo, hi):
                    last = nc.vector.tensor_tensor_reduce(
                        out=rows[:, j, :], in0=rows[:, j, :], in1=v_sb[:, 0:D], scale=1.0, scalar=0.0,
                        op0=ALU.mult, op1=ALU.add, accum_out=s_c[u % 2][:, j:j + 1])
                if hi == EIGHTH:
                    last.then_inc(c_dots, 1)

            def mask_scores(k, u):
                dve.wait_ge(h_dots, k + 1)
                nc.vector.scalar_tensor_tensor(out=s_hm[u % 2][:], in0=s_h[u % 2][:], scalar=bias_sb[:, 0:1],
                                               in1=cap[:, bass.ds(k * PAIRS, PAIRS)], op0=ALU.add,
                                               op1=ALU.min).then_inc(h_masked, 1)

            def batch_top(k, u):
                dve.wait_ge(h_turned, k + 1)
                nc.vector.tensor_reduce(top[u % 2][:], turned_ps[0:PAIRS, 0:P].rearrange("i (b h) -> i b h", b=2),
                                        AX_X, ALU.max).then_inc(top_found, 1)

            def place_top(k, u):
                dve.wait_ge(top_found, k + 1)
                nc.vector.tensor_tensor(
                    top_placed[u % 2][:], place_b[:],
                    top[u % 2][:].unsqueeze(1).unsqueeze(3).to_broadcast([PAIRS, PAIRS, 2, 8]),
                    ALU.mult).then_inc(top_spread, 1)

            def row_shift(k, u):
                dve.wait_ge(top_ready, k + 1)
                dve.wait_ge(c_dots, k + 1)
                nc.vector.scalar_tensor_tensor(out=shift[u % 2][:], in0=s_c[u % 2][:], scalar=top_ps[:, 0:1],
                                               in1=s_c[u % 2][:], op0=ALU.add, op1=ALU.subtract).then_inc(shifted, 1)

            def place_shift(k, u):
                dve.wait_ge(shifted, k + 1)
                nc.vector.tensor_tensor(
                    shift_placed[u % 2][:],
                    neg_place_c[:].unsqueeze(3).to_broadcast([P, PAIRS, 8, EIGHTH]),
                    shift[u % 2][:].unsqueeze(1).unsqueeze(1).to_broadcast([P, PAIRS, 8, EIGHTH]),
                    ALU.mult).then_inc(placed, 1)

            def invert_sums(k, u):
                dve.wait_ge(sums_ready, k + 1)
                nc.vector.reciprocal(inv_sum[u % 2][:], sum_ps[:, 0:PAIRS]).then_inc(inverted, 1)

            def row_scale(k, u):
                dve.wait_ge(inverted, k + 1)
                nc.vector.tensor_tensor(scale[u % 2][:], inv_sum[u % 2][:], keep[:, bass.ds(k * PAIRS, PAIRS)],
                                        ALU.mult).then_inc(scale_ready, 1)

            def set_up_rest():
                dve.wait_ge(v_ready, 2)
                nc.vector.tensor_copy(v_sb[:, 0:D], turned_ps[:, 0:D]).then_inc(v_copied, 1)
                nc.vector.tensor_copy(bias_sb[:], top_ps[:, 0:1]).then_inc(v_copied, 1)
                dve.wait_ge(masks_turned, 2 * MT)
                nc.vector.tensor_scalar(cap[:], user_ps[0][:, 0:NPAIR], 0.5, 2.0 * CAP, ALU.subtract,
                                        ALU.mult).then_inc(masks_ready, 1)
                nc.vector.tensor_copy(keep[:], user_ps[1][:, 0:NPAIR]).then_inc(masks_ready, 1)
                dve.wait_ge(consts_in, 64)
                dve.wait_ge(v_copied, 3)
                dve.wait_ge(masks_ready, 2)

            def step(k, u, behind, behind2):
                clicked_dots(k, u, 0, 3)
                if behind:
                    row_shift(k - 1, u - 1)
                clicked_dots(k, u, 3, 4)
                if behind:
                    place_shift(k - 1, u - 1)
                clicked_dots(k, u, 4, PAIRS)
                if not behind:
                    set_up_rest()
                cand_dots(k, u, 0, 1)
                mask_scores(k, u)
                cand_dots(k, u, 1, 4)
                batch_top(k, u)
                cand_dots(k, u, 4, 5)
                place_top(k, u)
                cand_dots(k, u, 5, 7)
                if behind2:
                    invert_sums(k - 2, u - 2)
                cand_dots(k, u, 7, EIGHTH)
                if behind2:
                    row_scale(k - 2, u - 2)

            for u in range(UNROLL):
                step(u, u, u >= 1, u >= 2)
            with dve.Fori(1, ROUNDS) as g:
                for u in range(UNROLL):
                    step(g * UNROLL + u, u, True, True)
            row_shift(CHUNKS - 1, 1)
            place_shift(CHUNKS - 1, 1)
            invert_sums(CHUNKS - 2, 0)
            row_scale(CHUNKS - 2, 0)
            invert_sums(CHUNKS - 1, 1)
            row_scale(CHUNKS - 1, 1)

        @block.tensor
        def _(pe):
            pe.wait_ge(w2_ready, 1)
            for t in range(KT):
                last = nc.tensor.matmul(exponent_ps[:, 0:D], w2_wide[:, t, :], w1_sb[:, t, D:2 * D],
                                        start=(t == 0), stop=(t == KT - 1))
            last.then_inc(v_ready, 1)
            for t in range(KT):
                nc.tensor.matmul(turned_ps[:, 0:D], w2_wide[:, t, :], w1_sb[:, t, 0:D],
                                 start=(t == 0), stop=(t == KT - 1))
            for t in range(KT):
                nc.tensor.matmul(top_ps[:, 0:1], w2_wide[:, t, :], b1_sb[:, t:t + 1], start=(t == 0), stop=False)
            pe.wait_ge(ones_ready, 1)
            nc.tensor.matmul(top_ps[:, 0:1], ones_row[:], b2_sb[:], start=False, stop=True).then_inc(v_ready, 1)
            pe.wait_ge(consts_in, 64)
            pe.wait_ge(masks_cast, 2)
            for n, flat in enumerate((hist_f, keep_f)):
                for t in range(MT):
                    nc.tensor.transpose(user_ps[n][:, t * P:(t + 1) * P], flat[:, t, :], ident[:]).then_inc(masks_turned, 1)
            pe.wait_ge(v_copied, 3)
            pe.wait_ge(masks_ready, 2)

            def turn_scores(k, u):
                pe.wait_ge(h_masked, k + 1)
                nc.tensor.transpose(turned_ps[0:PAIRS, 0:P], s_hm[u % 2][:], ident[:]).then_inc(h_turned, 1)

            def spread_top(k, u):
                pe.wait_ge(top_spread, k + 1)
                nc.tensor.matmul(top_ps[:, 0:1], top_placed[u % 2][:].rearrange("k i b q -> k (i b q)"),
                                 ones_col[0:PAIRS, :], start=True, stop=True).then_inc(top_ready, 1)

            def spread_exponents(k, u, again):
                pe.wait_ge(placed, k + 1)
                if again:
                    pe.wait_ge(exp_done, k)
                nc.tensor.matmul(exponent_ps[:], parity[:], shift_placed[u % 2][:].rearrange("p i q j -> p (i q j)"),
                                 start=True, stop=False)
                nc.tensor.matmul(exponent_ps[:], ident[:], s_hm[u % 2][:].unsqueeze(2).to_broadcast([P, PAIRS, C]),
                                 start=False, stop=True).then_inc(exponents, 1)

            def sums(k, u, again):
                pe.wait_ge(exp_done, k + 1)
                if again:
                    pe.wait_ge(inverted, k)
                for i in range(PAIRS):
                    last = nc.tensor.matmul(sum_ps[:, i:i + 1], weights[u % 2][:, i, :], ones_col[:], start=True, stop=True)
                last.then_inc(sums_ready, 1)

            def products(k, u, again):
                for n in range(BANKS):
                    if again:
                        pe.wait_ge(users_taken, BANKS * (k - 1) + n + 1)
                    for i in (2 * n, 2 * n + 1):
                        last = nc.tensor.matmul(user_ps[n][:, (i % 2) * D:(i % 2 + 1) * D], weights[u % 2][:, i, :],
                                                clicked_sb[u][:, i, :], start=True, stop=True)
                    last.then_inc(users_ready, 1)

            def step(k, u, behind1, behind2, behind3):
                if behind1:
                    spread_exponents(k - 1, u - 1, behind2)
                turn_scores(k, u)
                if behind2:
                    sums(k - 2, (u - 2) % UNROLL, behind3)
                spread_top(k, u)
                if behind2:
                    products(k - 2, (u - 2) % UNROLL, behind3)

            for u in range(UNROLL):
                step(u, u, u >= 1, u >= 2, u >= 3)
            with pe.Fori(1, ROUNDS) as g:
                for u in range(UNROLL):
                    step(g * UNROLL + u, u, True, True, True)
            spread_exponents(CHUNKS - 1, UNROLL - 1, True)
            for u in (UNROLL - 2, UNROLL - 1):
                sums(CHUNKS - UNROLL + u, u, True)
                products(CHUNKS - UNROLL + u, u, True)

        @block.scalar
        def _(act):
            def exponentials(k, u):
                act.wait_ge(exponents, k + 1)
                e = exponent_ps[:].rearrange("p (i c) -> p i c", c=C)
                nc.scalar.activation(weights[u % 2][0:H, :, 0:C], e[0:H], ACT.Exp)
                nc.scalar.activation(weights[u % 2][H:P, :, C:2 * C], e[H:P], ACT.Exp).then_inc(exp_done, 1)

            def take_users(k, u, again):
                act.wait_ge(scale_ready, k + 1)
                if again is not None:
                    act.wait_ge(stored[u], again)
                for n in range(BANKS):
                    act.wait_ge(users_ready, BANKS * k + n + 1)
                    for i in (2 * n, 2 * n + 1):
                        last = nc.scalar.activation(out_sb[u][:, i, :], user_ps[n][:, (i % 2) * D:(i % 2 + 1) * D],
                                                    ACT.Copy, scale=scale[u % 2][:, i:i + 1])
                    last.then_inc(users_taken, 1)

            act.wait_ge(ones_ready, 1)
            nc.scalar.activation(warm[:], ones_col[0:1, :], ACT.Exp)
            act.wait_ge(zeroed, 2)
            exponentials(0, 0)
            for u in range(UNROLL):
                exponentials(u + 1, (u + 1) % UNROLL)
                take_users(u, u, None)
            with act.Fori(1, ROUNDS - 1) as g:
                for u in range(UNROLL):
                    exponentials(g * UNROLL + u + 1, (u + 1) % UNROLL)
                    take_users(g * UNROLL + u, u, 16 * g)
            for u in range(UNROLL):
                k = (ROUNDS - 1) * UNROLL + u
                if k + 1 < CHUNKS:
                    exponentials(k + 1, u + 1)
                take_users(k, u, 16 * (ROUNDS - 1))


_INS = ["r_candidate_news_vector", "r_clicked_news_vector", "r_mask_cand", "r_mask_hist",
        "L0_rec_W1", "L0_rec_b1", "L0_rec_W2", "L0_rec_b2"]


def _placements():
    import numpy as np

    p = np.arange(P)
    ident = np.eye(P, dtype=np.float32)
    parity = (((p[:, None] // 8) % 2) == (p[None, :] // 64)).astype(np.float32)
    place_c = -((p[:, None, None] // 16 == np.arange(PAIRS)[None, :, None])
                & (p[:, None, None] % 8 == np.arange(8)[None, None, :])).astype(np.float32)
    place_b = np.zeros((PAIRS, PAIRS, 2, 8), np.float32)
    place_b[np.arange(PAIRS), np.arange(PAIRS)] = 1.0
    return {"identity": ident, "same_parity": parity, "place_candidate": place_c, "place_batch": place_b}


def kernel(**inputs):
    import numpy as np
    import concourse.bacc as bacc
    from concourse import mybir as _mybir
    from concourse.bass_utils import run_bass_kernel_spmd

    nc = bacc.Bacc("TRN2", target_bir_lowering=False, num_devices=1)
    arrays, args = {}, []
    for name, a in [(n, inputs[n]) for n in _INS] + list(_placements().items()):
        a = np.ascontiguousarray(a)
        arrays[f"in_{name}_dram"] = a
        args.append(nc.dram_tensor(f"in_{name}_dram", a.shape, _mybir.dt.from_np(a.dtype), kind="ExternalInput").ap())
    shape = inputs["r_candidate_news_vector"].shape
    args.append(nc.dram_tensor("out_0_dram", shape, F32, kind="ExternalOutput").ap())
    candidate_attention_kernel(nc, *args)
    r = run_bass_kernel_spmd(nc, [arrays], core_ids=[0])
    return r.results[0]["out_0_dram"]
```

```python
from contextlib import ExitStack

import concourse.bass as bass
from concourse import mybir

ALU = mybir.AluOpType
ACT = mybir.ActivationFunctionType
F32 = mybir.dt.float32
U8 = mybir.dt.uint8
BF16 = mybir.dt.bfloat16
AX_X = mybir.AxisListType.X

P = 128
PAIRS = 8
UNROLL = 8
CAND_RING = 4
GROUP = 4
SLACK = 64.0
CAP = 2.0 ** 126


def candidate_attention_kernel(
    nc: bass.Bass,
    cand: bass.AP,
    clicked: bass.AP,
    mask_cand: bass.AP,
    mask_hist: bass.AP,
    w1: bass.AP,
    b1: bass.AP,
    w2: bass.AP,
    b2: bass.AP,
    selections: bass.AP,
    out: bass.AP,
):
    B, C, D = cand.shape
    H = clicked.shape[1]
    HID = w1.shape[0]
    KT = HID // P
    NPAIR = B // 2
    CHUNKS = NPAIR // PAIRS
    ROUNDS = CHUNKS // UNROLL
    EIGHTH = 2 * C * PAIRS // P
    MT = NPAIR // P
    GROUPS = PAIRS // GROUP
    QUARTERS = PAIRS // 2
    ROW = D + D // 4
    ONES = 2
    assert 2 * H == P and 2 * C == P and 2 * D == 512 and PAIRS * C == 512

    clicked_v = clicked.rearrange("(k i b) h d -> k (b h) i d", i=PAIRS, b=2)
    out_v = out.rearrange("(k i b) c d -> k (b c) i d", i=PAIRS, b=2)
    cand_v = cand.rearrange("(k n) (q j) d -> k (n q) (j d)", n=2 * PAIRS, j=EIGHTH)

    with ExitStack() as ctx:
        def sb(name, shape, dt=F32):
            return ctx.enter_context(nc.sbuf_tensor(name, shape, dt))

        def ps(name):
            return ctx.enter_context(nc.psum_tensor(name, [P, 512], F32))

        def sem(name):
            return ctx.enter_context(nc.semaphore(name))

        clicked_sb = [sb(f"clicked{u}", [P, PAIRS, ROW]) for u in range(UNROLL)]
        cand_sb = [sb(f"cand{u}", [P, EIGHTH, D]) for u in range(CAND_RING)]
        out_sb = [sb(f"out{u}", [P, PAIRS, D]) for u in range(UNROLL)]

        selection_sb = sb("selection_sb", [P, 2 * P + QUARTERS + 16])
        ident = selection_sb[:, 0:P]
        parity = selection_sb[:, P:2 * P]
        quarter_of = selection_sb[:, 2 * P:2 * P + QUARTERS]
        neg_place_c = selection_sb[:, 2 * P + QUARTERS:].rearrange("p (i q) -> p i q", i=2)
        gather = sb("gather", [P, QUARTERS, P])
        other = sb("other", [P, P])
        ones_row = sb("ones_row", [1, P])
        ones_col = sb("ones_col", [P, 1])
        warm = sb("warm", [1, 1])
        w1_sb = sb("w1_sb", [P, KT, 2 * D])
        w2_sb = sb("w2_sb", [P, KT])
        w2_wide = sb("w2_wide", [P, KT, P])
        b1_sb = sb("b1_sb", [P, KT])
        b2_sb = sb("b2_sb", [1, 1])
        v_sb = sb("v_sb", [P, 2 * D])
        bias_sb = sb("bias_sb", [P, 1])
        hist_u8 = sb("hist_u8", [P, MT, P], U8)
        keep_u8 = sb("keep_u8", [P, MT, P], U8)
        hist_f = sb("hist_f", [P, MT, P])
        keep_f = sb("keep_f", [P, MT, P])
        cap = sb("cap", [P, NPAIR])
        keep = sb("keep", [P, NPAIR])

        product = sb("product", [P, PAIRS, D], BF16)
        s_h = [sb(f"s_h{u}", [P, PAIRS]) for u in range(2)]
        s_hm = [sb(f"s_hm{u}", [P, PAIRS, P // PAIRS]) for u in range(2)]
        s_c = [sb(f"s_c{u}", [P, EIGHTH]) for u in range(2)]
        top = [sb(f"top{u}", [P, 1]) for u in range(2)]
        ceiling = [sb(f"ceiling{u}", [P, 1]) for u in range(2)]
        raw_shift = [sb(f"raw_shift{u}", [P, EIGHTH]) for u in range(2)]
        shift = [sb(f"shift{u}", [P, EIGHTH]) for u in range(2)]
        shift_placed = [sb(f"shift_placed{u}", [P, 2, 8, EIGHTH]) for u in range(2)]
        weights = [sb(f"weights{u}", [P, PAIRS, P]) for u in range(2)]
        inv_sum = [sb(f"inv_sum{n}", [P, GROUP]) for n in range(GROUPS)]
        scale = [sb(f"scale{n}", [P, GROUP]) for n in range(GROUPS)]

        user_ps = ctx.enter_context(nc.psum_tensor("user_ps", [P, GROUP, 512], F32))
        exponent_ps = ps("exponent_ps")
        turned_ps = ps("turned_ps")
        bias_ps = ps("bias_ps")

        clicked_in = [sem(f"clicked_in{u}") for u in range(UNROLL)]
        cand_in = [sem(f"cand_in{u}") for u in range(CAND_RING)]
        stored = [sem(f"stored{u}") for u in range(UNROLL)]
        weights_in = sem("weights_in")
        consts_in = sem("consts_in")
        masks_in = sem("masks_in")
        zeroed = sem("zeroed")
        rows_ready = sem("rows_ready")
        ones_ready = sem("ones_ready")
        gather_ready = sem("gather_ready")
        w2_ready = sem("w2_ready")
        v_ready = sem("v_ready")
        v_copied = sem("v_copied")
        masks_cast = sem("masks_cast")
        masks_turned = sem("masks_turned")
        masks_ready = sem("masks_ready")
        h_dots = sem("h_dots")
        c_dots = sem("c_dots")
        h_masked = sem("h_masked")
        h_turned = sem("h_turned")
        top_found = sem("top_found")
        ceiling_found = sem("ceiling_found")
        shifted = sem("shifted")
        shift_held = sem("shift_held")
        placed = sem("placed")
        exponents = sem("exponents")
        exp_done = sem("exp_done")
        inverted = sem("inverted")
        scale_ready = sem("scale_ready")
        users_ready = sem("users_ready")
        users_taken = sem("users_taken")

        block = ctx.enter_context(nc.Block())

        @block.sync
        def _(sp):
            sp.dma_start(w1_sb[:], w1.rearrange("(p t) n -> p t n", t=KT)).then_inc(weights_in, 16)
            sp.dma_start(w2_sb[:], w2.rearrange("a (p t) -> (a p) t", t=KT)).then_inc(weights_in, 16)
            sp.dma_start(b1_sb[:], b1.rearrange("(p t) -> p t", t=KT)).then_inc(weights_in, 16)
            sp.dma_start(b2_sb[:], b2.rearrange("(a n) -> a n", a=1)).then_inc(weights_in, 16)

            def load_clicked(k, u, again):
                if again:
                    sp.wait_ge(users_ready, GROUPS * (k - UNROLL + 1))
                sp.dma_start(clicked_sb[u][:, :, 0:D], clicked_v[k]).then_inc(clicked_in[u], 16)

            def load_cand(k, u, again):
                if again:
                    sp.wait_ge(c_dots, k - CAND_RING + 1)
                sp.dma_start(cand_sb[u % CAND_RING][:], cand_v[k]).then_inc(cand_in[u % CAND_RING], 16)

            def store(k, u):
                sp.wait_ge(users_taken, PAIRS * (k + 1))
                sp.dma_start(out_v[k], out_sb[u][:]).then_inc(stored[u], 16)

            load_clicked(0, 0, False)
            for flat, mask in ((hist_u8, mask_hist), (keep_u8, mask_cand)):
                sp.dma_start(flat[:], mask.rearrange("(t p b) h -> p t (b h)", p=P, b=2)).then_inc(masks_in, 16)
            sp.dma_start(selection_sb[:], selections).then_inc(consts_in, 16)
            load_cand(0, 0, False)
            for u in range(1, UNROLL):
                load_clicked(u, u, False)
                load_cand(u, u, u >= CAND_RING)
            with sp.Fori(0, ROUNDS - 1) as g:
                for u in range(UNROLL):
                    k = g * UNROLL + u
                    load_clicked(k + UNROLL, u, True)
                    load_cand(k + UNROLL, u, True)
                    store(k, u)
            for u in range(UNROLL):
                store(CHUNKS - UNROLL + u, u)
            for u in range(UNROLL):
                sp.wait_ge(stored[u], 16 * ROUNDS)

        @block.gpsimd
        def _(pool):
            for u in range(2):
                nc.gpsimd.memset(weights[u][:], 0.0).then_inc(zeroed, 1)
            for u in range(UNROLL):
                nc.gpsimd.memset(clicked_sb[u][:, :, D:D + ONES], 1.0).then_inc(ones_ready, 1)
            pool.wait_ge(masks_in, 32)
            nc.gpsimd.tensor_copy(hist_f[:], hist_u8[:]).then_inc(masks_cast, 1)
            nc.gpsimd.tensor_copy(keep_f[:], keep_u8[:]).then_inc(masks_cast, 1)
            pool.wait_ge(consts_in, 16)
            nc.gpsimd.tensor_tensor(gather[:], parity.unsqueeze(1).to_broadcast([P, QUARTERS, P]),
                                    quarter_of.unsqueeze(2).to_broadcast([P, QUARTERS, P]), ALU.mult).then_inc(gather_ready, 1)
            nc.gpsimd.tensor_scalar(other[:], parity, 1.0, CAP, ALU.subtract, ALU.mult).then_inc(gather_ready, 1)

        @block.vector
        def _(dve):
            nc.vector.memset(ones_row[:], 1.0)
            nc.vector.memset(ones_col[:], 1.0).then_inc(rows_ready, 1)
            dve.wait_ge(weights_in, 64)
            nc.vector.tensor_copy(w2_wide[:], w2_sb[:].unsqueeze(2).to_broadcast([P, KT, P])).then_inc(w2_ready, 1)
            dve.wait_ge(v_ready, 1)
            nc.vector.tensor_copy(v_sb[:, D:2 * D], exponent_ps[:, 0:D]).then_inc(v_copied, 1)
            dve.wait_ge(v_copied, 1)

            def slot_filled(k, u, ring):
                return (k - u % ring) * (16 // ring) + 16

            def clicked_dots(k, u, lo, hi):
                if lo == 0:
                    dve.wait_ge(clicked_in[u], slot_filled(k, u, UNROLL))
                for j in range(lo, hi):
                    last = nc.vector.tensor_tensor_reduce(
                        out=product[:, j, :], in0=clicked_sb[u][:, j, 0:D], in1=v_sb[:, D:2 * D], scale=1.0, scalar=0.0,
                        op0=ALU.mult, op1=ALU.add, accum_out=s_h[u % 2][:, j:j + 1])
                if hi == PAIRS:
                    last.then_inc(h_dots, 1)

            def cand_dots(k, u, lo, hi):
                if lo == 0:
                    dve.wait_ge(cand_in[u % CAND_RING], slot_filled(k, u, CAND_RING))
                rows = cand_sb[u % CAND_RING]
                for j in range(lo, hi):
                    last = nc.vector.tensor_tensor_reduce(
                        out=rows[:, j, :], in0=rows[:, j, :], in1=v_sb[:, 0:D], scale=1.0, scalar=0.0,
                        op0=ALU.mult, op1=ALU.add, accum_out=s_c[u % 2][:, j:j + 1])
                if hi == EIGHTH:
                    last.then_inc(c_dots, 1)

            def mask_scores(k, u):
                dve.wait_ge(h_dots, k + 1)
                wide = [P, PAIRS, P // PAIRS]
                nc.vector.scalar_tensor_tensor(
                    out=s_hm[u % 2][:], in0=s_h[u % 2][:].unsqueeze(2).to_broadcast(wide), scalar=bias_sb[:, 0:1],
                    in1=cap[:, bass.ds(k * PAIRS, PAIRS)].unsqueeze(2).to_broadcast(wide), op0=ALU.add,
                    op1=ALU.min).then_inc(h_masked, 1)

            def batch_top(k, u):
                dve.wait_ge(h_turned, k + 1)
                nc.vector.tensor_reduce(top[u % 2][:], turned_ps[:, 0:P], AX_X, ALU.max).then_inc(top_found, 1)

            def shift_ceiling(k, u):
                dve.wait_ge(top_found, k + 1)
                nc.vector.tensor_scalar(ceiling[u % 2][:], top[u % 2][:], SLACK, None,
                                        ALU.add).then_inc(ceiling_found, 1)

            def row_shift(k, u):
                dve.wait_ge(top_found, k + 1)
                dve.wait_ge(c_dots, k + 1)
                nc.vector.scalar_tensor_tensor(out=raw_shift[u % 2][:], in0=s_c[u % 2][:], scalar=top[u % 2][:, 0:1],
                                               in1=s_c[u % 2][:], op0=ALU.add, op1=ALU.subtract).then_inc(shifted, 1)

            def hold_shift(k, u):
                dve.wait_ge(ceiling_found, k + 1)
                dve.wait_ge(shifted, k + 1)
                nc.vector.tensor_scalar(shift[u % 2][:], raw_shift[u % 2][:], top[u % 2][:, 0:1],
                                        ceiling[u % 2][:, 0:1], ALU.max, ALU.min).then_inc(shift_held, 1)

            def place_shift(k, u):
                dve.wait_ge(shift_held, k + 1)
                nc.vector.tensor_tensor(
                    shift_placed[u % 2][:],
                    neg_place_c.unsqueeze(3).to_broadcast([P, 2, 8, EIGHTH]),
                    shift[u % 2][:].unsqueeze(1).unsqueeze(1).to_broadcast([P, 2, 8, EIGHTH]),
                    ALU.mult).then_inc(placed, 1)

            def invert_sums(k, n):
                dve.wait_ge(users_ready, GROUPS * k + n + 1)
                nc.vector.reciprocal(inv_sum[n][:], user_ps[:, :, D]).then_inc(inverted, 1)

            def row_scale(k, n):
                dve.wait_ge(inverted, GROUPS * k + n + 1)
                nc.vector.tensor_tensor(scale[n][:], inv_sum[n][:], keep[:, bass.ds(k * PAIRS + n * GROUP, GROUP)],
                                        ALU.mult).then_inc(scale_ready, 1)

            def set_up_rest():
                dve.wait_ge(v_ready, 2)
                nc.vector.tensor_copy(v_sb[:, 0:D], turned_ps[:, 0:D]).then_inc(v_copied, 1)
                nc.vector.tensor_copy(bias_sb[:], bias_ps[:, 0:1]).then_inc(v_copied, 1)
                dve.wait_ge(masks_turned, 2 * MT)
                nc.vector.tensor_scalar(cap[:], user_ps[:, 0, 0:NPAIR], 0.5, 2.0 * CAP, ALU.subtract,
                                        ALU.mult).then_inc(masks_ready, 1)
                nc.vector.tensor_copy(keep[:], user_ps[:, 1, 0:NPAIR]).then_inc(masks_ready, 1)
                dve.wait_ge(consts_in, 16)
                dve.wait_ge(v_copied, 3)
                dve.wait_ge(masks_ready, 2)

            def step(k, u, behind, behind2):
                clicked_dots(k, u, 0, 2)
                if behind:
                    row_shift(k - 1, u - 1)
                clicked_dots(k, u, 2, 3)
                if behind:
                    hold_shift(k - 1, u - 1)
                clicked_dots(k, u, 3, 4)
                if behind:
                    place_shift(k - 1, u - 1)
                clicked_dots(k, u, 4, 5)
                if behind2:
                    invert_sums(k - 2, 0)
                clicked_dots(k, u, 5, 6)
                if behind2:
                    row_scale(k - 2, 0)
                clicked_dots(k, u, 6, PAIRS)
                if not behind:
                    set_up_rest()
                cand_dots(k, u, 0, 1)
                mask_scores(k, u)
                cand_dots(k, u, 1, 5)
                batch_top(k, u)
                cand_dots(k, u, 5, 6)
                shift_ceiling(k, u)
                cand_dots(k, u, 6, 7)
                if behind2:
                    invert_sums(k - 2, 1)
                cand_dots(k, u, 7, EIGHTH)
                if behind2:
                    row_scale(k - 2, 1)

            for u in range(UNROLL):
                step(u, u, u >= 1, u >= 2)
            with dve.Fori(1, ROUNDS) as g:
                for u in range(UNROLL):
                    step(g * UNROLL + u, u, True, True)
            row_shift(CHUNKS - 1, 1)
            hold_shift(CHUNKS - 1, 1)
            place_shift(CHUNKS - 1, 1)
            for k in (CHUNKS - 2, CHUNKS - 1):
                for n in range(GROUPS):
                    invert_sums(k, n)
                    row_scale(k, n)

        @block.tensor
        def _(pe):
            pe.wait_ge(w2_ready, 1)
            for t in range(KT):
                last = nc.tensor.matmul(exponent_ps[:, 0:D], w2_wide[:, t, :], w1_sb[:, t, D:2 * D],
                                        start=(t == 0), stop=(t == KT - 1))
            last.then_inc(v_ready, 1)
            for t in range(KT):
                nc.tensor.matmul(turned_ps[:, 0:D], w2_wide[:, t, :], w1_sb[:, t, 0:D],
                                 start=(t == 0), stop=(t == KT - 1))
            for t in range(KT):
                nc.tensor.matmul(bias_ps[:, 0:1], w2_wide[:, t, :], b1_sb[:, t:t + 1], start=(t == 0), stop=False)
            pe.wait_ge(rows_ready, 1)
            nc.tensor.matmul(bias_ps[:, 0:1], ones_row[:], b2_sb[:], start=False, stop=True).then_inc(v_ready, 1)
            pe.wait_ge(consts_in, 16)
            pe.wait_ge(masks_cast, 2)
            for n, flat in enumerate((hist_f, keep_f)):
                for t in range(MT):
                    nc.tensor.transpose(user_ps[:, n, t * P:(t + 1) * P], flat[:, t, :], ident).then_inc(masks_turned, 1)
            pe.wait_ge(v_copied, 3)
            pe.wait_ge(masks_ready, 2)
            pe.wait_ge(gather_ready, 2)

            def turn_scores(k, u):
                pe.wait_ge(h_masked, k + 1)
                nc.tensor.matmul(turned_ps[:, 0:P], s_hm[u % 2][:].rearrange("p i n -> p (i n)"), ident,
                                 start=True, stop=False)
                nc.tensor.matmul(turned_ps[:, 0:P], ident, other[:], start=False, stop=True).then_inc(h_turned, 1)

            def spread_exponents(k, u, again):
                if again:
                    pe.wait_ge(exp_done, k)
                nc.tensor.matmul(exponent_ps[:], ident, s_hm[u % 2][:, :, 0:1].to_broadcast([P, PAIRS, C]),
                                 start=True, stop=False)
                pe.wait_ge(placed, k + 1)
                for r in range(QUARTERS):
                    last = nc.tensor.matmul(exponent_ps[:, r * 2 * C:(r + 1) * 2 * C], gather[:, r, :],
                                            shift_placed[u % 2][:].rearrange("p i q j -> p (i q j)"),
                                            start=False, stop=(r == QUARTERS - 1))
                last.then_inc(exponents, 1)

            def products(k, u, n, banks_used=True):
                pe.wait_ge(exp_done, k + 1)
                for b in range(GROUP):
                    i = n * GROUP + b
                    if banks_used:
                        pe.wait_ge(users_taken, PAIRS * k + i - GROUP + 1)
                    last = nc.tensor.matmul(user_ps[:, b, 0:D + ONES], weights[u % 2][:, i, :],
                                            clicked_sb[u][:, i, 0:D + ONES], start=True, stop=True)
                last.then_inc(users_ready, 1)

            def step(k, u, behind1, behind2, behind3):
                if behind2:
                    products(k - 2, (u - 2) % UNROLL, 0, behind3)
                if behind1:
                    spread_exponents(k - 1, u - 1, behind2)
                turn_scores(k, u)
                if behind2:
                    products(k - 2, (u - 2) % UNROLL, 1)

            pe.wait_ge(ones_ready, UNROLL)
            for u in range(UNROLL):
                step(u, u, u >= 1, u >= 2, u >= 3)
            with pe.Fori(1, ROUNDS) as g:
                for u in range(UNROLL):
                    step(g * UNROLL + u, u, True, True, True)
            products(CHUNKS - 2, UNROLL - 2, 0)
            spread_exponents(CHUNKS - 1, UNROLL - 1, True)
            products(CHUNKS - 2, UNROLL - 2, 1)
            products(CHUNKS - 1, UNROLL - 1, 0)
            products(CHUNKS - 1, UNROLL - 1, 1)

        @block.scalar
        def _(act):
            def exponentials(k, u):
                act.wait_ge(exponents, k + 1)
                e = exponent_ps[:].rearrange("p (i c) -> p i c", c=C)
                nc.scalar.activation(weights[u % 2][0:H, :, 0:C], e[0:H], ACT.Exp)
                nc.scalar.activation(weights[u % 2][H:P, :, C:2 * C], e[H:P], ACT.Exp).then_inc(exp_done, 1)

            def take_users(k, u, n, again):
                act.wait_ge(scale_ready, GROUPS * k + n + 1)
                if again is not None and n == 0:
                    act.wait_ge(stored[u], again)
                for b in range(GROUP):
                    nc.scalar.activation(out_sb[u][:, n * GROUP + b, :], user_ps[:, b, 0:D], ACT.Copy,
                                         scale=scale[n][:, b:b + 1]).then_inc(users_taken, 1)

            act.wait_ge(rows_ready, 1)
            nc.scalar.activation(warm[:], ones_col[0:1, :], ACT.Exp)
            act.wait_ge(zeroed, 2)
            exponentials(0, 0)

            def step(k, u, again, last=False):
                take_users(k, u, 0, again)
                if not last:
                    exponentials(k + 1, u + 1)
                take_users(k, u, 1, again)

            for u in range(UNROLL):
                step(u, u, None)
            with act.Fori(1, ROUNDS - 1) as g:
                for u in range(UNROLL):
                    step(g * UNROLL + u, u, 16 * g)
            for u in range(UNROLL):
                step((ROUNDS - 1) * UNROLL + u, u, 16 * (ROUNDS - 1), u == UNROLL - 1)


_INS = ["r_candidate_news_vector", "r_clicked_news_vector", "r_mask_cand", "r_mask_hist",
        "L0_rec_W1", "L0_rec_b1", "L0_rec_W2", "L0_rec_b2"]


def _selections():
    import numpy as np

    p = np.arange(P)
    ident = np.eye(P)
    parity = p[:, None] // 8 % 2 == p[None, :] // 64
    quarter = p[:, None] // 32 == np.arange(PAIRS // 2)[None, :]
    n = np.arange(16)[None, :]
    place = (p[:, None] // 16 % 2 == n // 8) & (p[:, None] % 8 == n % 8)
    return np.concatenate([ident, parity, quarter, -1.0 * place], axis=1).astype(np.float32)


def kernel(**inputs):
    import numpy as np
    import concourse.bacc as bacc
    from concourse import mybir as _mybir
    from concourse.bass_utils import run_bass_kernel_spmd

    nc = bacc.Bacc("TRN2", target_bir_lowering=False, num_devices=1)
    arrays, args = {}, []
    for name, a in [(n, inputs[n]) for n in _INS] + [("selections", _selections())]:
        a = np.ascontiguousarray(a)
        arrays[f"in_{name}_dram"] = a
        args.append(nc.dram_tensor(f"in_{name}_dram", a.shape, _mybir.dt.from_np(a.dtype), kind="ExternalInput").ap())
    shape = inputs["r_candidate_news_vector"].shape
    args.append(nc.dram_tensor("out_0_dram", shape, F32, kind="ExternalOutput").ap())
    candidate_attention_kernel(nc, *args)
    r = run_bass_kernel_spmd(nc, [arrays], core_ids=[0])
    return r.results[0]["out_0_dram"]
```
